# Optimizing a Trainium2 kernel written in Bass

```python
import numpy as np
import jax
import jax.numpy as jnp

def _softmax(x, axis=-1):
    return jax.nn.softmax(x, axis=axis)

def _gelu(x):
    return jax.nn.gelu(x, approximate=True)

def _silu(x):
    return jax.nn.silu(x)

def _sigmoid(x):
    return jax.nn.sigmoid(x)

def _layernorm(x, axis=-1, eps=1e-05):
    m = jnp.mean(x, axis=axis, keepdims=True)
    v = jnp.var(x, axis=axis, keepdims=True)
    return (x - m) / jnp.sqrt(v + eps)

def _scatter_add(tgt, idx, src, axis=0):
    return tgt.at[idx].add(src)

def _segment_sum(src, seg, n):
    return jax.ops.segment_sum(src, seg, n)
kernel_name = 'mk_adaln_ffn_d1_seqx_r4_8507db'

def setup_inputs(seed: int=0):
    np.random.seed(seed)
    _w = jnp.asarray

    def _rec_inputs():
        import jax
        import jax.numpy as jnp
        _rk = jax.random.key(seed)
        x = 7.22e-05 + 1 * jax.random.normal(jax.random.fold_in(_rk, 1), (8, 256, 1024), jnp.float32)
        _lenS = 256 - jax.random.randint(jax.random.fold_in(_rk, 7), (8,), 0, max(1, 256 // 4) + 1, jnp.int32)
        _lenS2 = 256 - jax.random.randint(jax.random.fold_in(_rk, 8), (8,), 0, max(1, 256 // 4) + 1, jnp.int32)
        itok_B_2_6 = jax.random.randint(jax.random.fold_in(_rk, 11), (8,), 2, 7, jnp.int32)
        return (x, itok_B_2_6)
    x, itok_B_2_6 = _rec_inputs()

    def _L0_cond_setup():
        import jax, jax.numpy as jnp
        import numpy as np
        B, N, H, F = (4, 128, 1024, 2752)
        L, R, RANK = (1, 16, 16)
        SCALE = 0.5
        key = jax.random.key(seed)
        ks = jax.random.split(key, 12)
        nrm = lambda k, shape, fan: jax.random.normal(k, shape, jnp.float32) * fan ** (-0.5)
        inp = {'x': jax.random.normal(ks[0], (B, N, H), jnp.float32), 'W_gate': nrm(ks[1], (F, H), H), 'W_up': nrm(ks[2], (F, H), H), 'W_down': nrm(ks[3], (H, F), F), 'A_gate': nrm(ks[4], (L, R, RANK, H), H), 'B_gate': nrm(ks[5], (L, R, F, RANK), RANK), 'A_up': nrm(ks[6], (L, R, RANK, H), H), 'B_up': nrm(ks[7], (L, R, F, RANK), RANK), 'A_down': nrm(ks[8], (L, R, RANK, F), F), 'B_down': nrm(ks[9], (L, R, H, RANK), RANK), 'lora_indices': jax.random.randint(ks[10], (B,), 0, R), 'layer_idx': 0}
        return inp
    _L0_cond_all = _L0_cond_setup()
    _L0_cond_in = {k: v for k, v in _L0_cond_all.items() if k in ('W_gate', 'W_up', 'W_down', 'A_gate', 'B_gate', 'A_up', 'B_up', 'A_down', 'B_down')}
    del _L0_cond_all

    def _L0_ffn_setup():
        import jax, jax.numpy as jnp
        import numpy as np
        B, S, D_IN, D_OUT = (2, 512, 1024, 1024)
        E, K, R = (8, 2, 16)
        SCALING = 32.0 / 16.0
        key = jax.random.key(seed)
        ks = jax.random.split(key, 6)
        x = jax.random.normal(ks[0], (B, S, D_IN), dtype=jnp.float32)
        gate_w = jax.random.normal(ks[1], (E, D_IN), dtype=jnp.float32) * 0.02
        base_w = jax.random.normal(ks[2], (D_OUT, D_IN), dtype=jnp.float32) * 0.02
        base_b = jax.random.normal(ks[3], (D_OUT,), dtype=jnp.float32) * 0.02
        lora_A = jax.random.normal(ks[4], (E, R, D_IN), dtype=jnp.float32) * 0.02
        lora_B = jax.random.normal(ks[5], (E, D_OUT, R), dtype=jnp.float32) * 0.02
        return {'x': x, 'gate_w': gate_w, 'base_w': base_w, 'base_b': base_b, 'lora_A': lora_A, 'lora_B': lora_B}
    _L0_ffn_all = _L0_ffn_setup()
    _L0_ffn_in = {k: v for k, v in _L0_ffn_all.items() if k in ('gate_w', 'base_w', 'base_b', 'lora_A', 'lora_B')}
    del _L0_ffn_all
    return {'x': x, 'itok_B_2_6': itok_B_2_6, 'L0_cond_W_gate': _L0_cond_in['W_gate'], 'L0_cond_W_up': _L0_cond_in['W_up'], 'L0_cond_W_down': _L0_cond_in['W_down'], 'L0_cond_A_gate': _L0_cond_in['A_gate'], 'L0_cond_B_gate': _L0_cond_in['B_gate'], 'L0_cond_A_up': _L0_cond_in['A_up'], 'L0_cond_B_up': _L0_cond_in['B_up'], 'L0_cond_A_down': _L0_cond_in['A_down'], 'L0_cond_B_down': _L0_cond_in['B_down'], 'L0_ffn_gate_w': _L0_ffn_in['gate_w'], 'L0_ffn_base_w': _L0_ffn_in['base_w'], 'L0_ffn_base_b': _L0_ffn_in['base_b'], 'L0_ffn_lora_A': _L0_ffn_in['lora_A'], 'L0_ffn_lora_B': _L0_ffn_in['lora_B']}

def reference(x, itok_B_2_6, L0_cond_W_gate, L0_cond_W_up, L0_cond_W_down, L0_cond_A_gate, L0_cond_B_gate, L0_cond_A_up, L0_cond_B_up, L0_cond_A_down, L0_cond_B_down, L0_ffn_gate_w, L0_ffn_base_w, L0_ffn_base_b, L0_ffn_lora_A, L0_ffn_lora_B):
    import jax
    import jax.numpy as jnp

    def _L0_cond_ref(x, W_gate, W_up, W_down, A_gate, B_gate, A_up, B_up, A_down, B_down, lora_indices, layer_idx):
        import jax, jax.numpy as jnp
        import numpy as np
        B, N, H, F = (4, 128, 1024, 2752)
        L, R, RANK = (1, 16, 16)
        SCALE = 0.5

        def lora_add(base, inp, A, B):
            Ab = A[layer_idx][lora_indices]
            Bb = B[layer_idx][lora_indices]
            t = jnp.einsum('bri,bni->bnr', Ab, inp)
            return base + jnp.einsum('bor,bnr->bno', Bb, t) * SCALE
        gate = lora_add(jnp.einsum('bnh,fh->bnf', x, W_gate), x, A_gate, B_gate)
        up = lora_add(jnp.einsum('bnh,fh->bnf', x, W_up), x, A_up, B_up)
        act = jax.nn.silu(gate) * up
        down = lora_add(jnp.einsum('bnf,hf->bnh', act, W_down), act, A_down, B_down)
        return down

    def _L0_ffn_ref(x, gate_w, base_w, base_b, lora_A, lora_B):
        import jax, jax.numpy as jnp
        import numpy as np
        B, S, D_IN, D_OUT = (2, 512, 1024, 1024)
        E, K, R = (8, 2, 16)
        SCALING = 32.0 / 16.0
        gate_logits = jnp.einsum('bsd,ed->bse', x, gate_w)
        weights, selected = jax.lax.top_k(gate_logits, K)
        weights = jax.nn.softmax(weights.astype(jnp.float32), axis=2).astype(x.dtype)
        result = jnp.einsum('bsd,od->bso', x, base_w) + base_b
        w_full = jnp.sum(jax.nn.one_hot(selected, E, dtype=x.dtype) * weights[..., None], axis=2)
        low = jnp.einsum('bsd,erd->ebsr', x, lora_A)
        lora_out = jnp.einsum('ebsr,eor,bse->bso', low, lora_B, w_full)
        result = result + SCALING * lora_out
        return result
    x = x + _L0_ffn_ref(_L0_cond_ref(x, L0_cond_W_gate, L0_cond_W_up, L0_cond_W_down, L0_cond_A_gate, L0_cond_B_gate, L0_cond_A_up, L0_cond_B_up, L0_cond_A_down, L0_cond_B_down, itok_B_2_6, 0), L0_ffn_gate_w, L0_ffn_base_w, L0_ffn_base_b, L0_ffn_lora_A, L0_ffn_lora_B)
    return x

_drawn_inputs = setup_inputs


def setup_inputs(seed=0):
    import zlib

    import numpy as np

    out = dict(_drawn_inputs(seed))
    spreads = {}
    factors = {'L0_ffn_base_b': 3.729}
    for name, (base, spread) in spreads.items():
        noise = np.random.default_rng([zlib.crc32(name.encode()), seed]).standard_normal(out[name].shape)
        drawn = base * np.exp(spread * noise) if base else spread * noise
        out[name] = jnp.asarray(drawn.astype(out[name].dtype))
    for name, factor in factors.items():
        out[name] = (out[name] * factor).astype(out[name].dtype)
    return out
```

```python
import concourse.bass as bass
import numpy as np
from concourse import mybir
from contextlib import ExitStack

P = 128
BATCH, SEQ, H = 8, 256, 1024
F = 2752
IDS, RANK = 16, 16
EXPERTS = 8
ER = EXPERTS * RANK
TOK = 512
CHUNKS = BATCH * SEQ // TOK
KT = H // P
FT = F // P
FREM = F - FT * P
GROUP = 3
GROUPS = FT // GROUP
SLAB = KT * P

S_AGU, S_REM = 0, 1
S_GATE = 2
S_ADN = S_GATE + 2 * FT
S_DOWN = S_ADN + 1
S_LOW = S_DOWN + 3 * KT
S_BASE = S_LOW + 1
SLABS = S_BASE + KT
RING = 3
W_REM, W_GATE, W_DOWN = 0, 1, 1 + 2 * FT
W_LOW = W_DOWN + 3 * KT
W_BASE = W_LOW + 1

LB = 1 + FT + KT + 1
B_LOADS = 1 + GROUPS + 2
GU_EVAC = FT + 3
DN = KT + 2
ROUTE = 11


def build(nc, w_stream, a_gu, a_dn, b_gu, b_dn, lora_b, gate_w, bias, x_t, idx, c_gu, c_dn, ident, cols, sum16, iota, out):
    fp32, f32r, i32, u32 = mybir.dt.float32, mybir.dt.float32r, mybir.dt.int32, mybir.dt.uint32
    ALU, ACT = mybir.AluOpType, mybir.ActivationFunctionType
    ctx = ExitStack()
    with ctx:
        def sb(name, shape, dt):
            return ctx.enter_context(nc.sbuf_tensor(name, shape, dt))

        def sem(name):
            return ctx.enter_context(nc.semaphore(name))

        xs = sb("xs", [P, 2, KT, TOK], f32r)
        dn = sb("dn", [P, 2, KT, TOK], f32r)
        act = sb("act", [P, 2, FT, TOK], f32r)
        act_rem = sb("act_rem", [P, TOK], f32r)
        slab = sb("slab", [P, RING, 2 * SLAB], f32r)
        raw = sb("raw", [P, RING, SLAB], fp32)
        b_raw = sb("b_raw", [P, 1024], fp32)
        b_st = sb("b_st", [P, 1024], f32r)
        r_mv = sb("r_mv", [P, 2, TOK], f32r)
        phl = sb("phl", [P, 2, TOK], f32r)
        x_stage = sb("x_stage", [P, 2, TOK], fp32)
        res = sb("res", [P, 2, TOK], fp32)
        s_sb = sb("s_sb", [P, TOK], fp32)
        a_sb = sb("a_sb", [P, TOK], fp32)
        route = sb("route", [P, 4, EXPERTS, RANK], fp32)
        gl_sb = route[0:2 * EXPERTS].rearrange("p a e r -> p (a e r)")
        cgu = sb("cgu", [P, 2, P], f32r)
        cdn = sb("cdn", [64, P], f32r)
        idn = sb("idn", [P, P], fp32)
        gw = sb("gw", [P, KT, 2 * EXPERTS], f32r)
        bias_sb = sb("bias_sb", [P, KT], fp32)
        col = sb("col", [P, 2], fp32)
        s16 = sb("s16", [2 * EXPERTS, EXPERTS], fp32)
        io = sb("io", [P, EXPERTS], fp32)
        lg = sb("lg", [P, 4, 8], fp32)
        mx = sb("mx", [P, 4, 8], fp32)
        mi = sb("mi", [P, 4, 8], u32)
        mf = sb("mf", [P, 4, 8], fp32)
        eq = sb("eq", [P, 2, 4, 8], fp32)
        wt = sb("wt", [P, 5, 4], fp32)
        ids = sb("ids", [1, BATCH + 2], i32)
        idc = sb("idc", [1, BATCH + 2], i32)
        idf = sb("idf", [1, 2, BATCH + 2], fp32)

        bank = [ctx.enter_context(nc.psum_tensor(f"bank{i}", [P, TOK], fp32)) for i in range(8)]
        ps_p, ps_rem, ps_t = bank[2], bank[3], (bank[0], bank[1])
        ps_pd, ps_td = bank[6], bank[7]
        ps_low, ps_gl, ps_lg, ps_wt = bank[2], bank[3], bank[0], bank[1]

        const_full = sem("const_full")
        const_ready, const_hi, id_step = sem("const_ready"), sem("const_hi"), sem("id_step")
        raw_full = [sem(f"raw_full{i}") for i in range(RING)]
        low_full = sem("low_full")
        hi_done, slab_ready, slab_used = sem("hi_done"), sem("slab_ready"), sem("slab_used")
        b_full, b_hi, b_ready = sem("b_full"), sem("b_hi"), sem("b_ready")
        xst_full = [sem("xst_full0"), sem("xst_full1")]
        x_hi, x_ready = sem("x_hi"), sem("x_ready")
        p_hi, p_ready, t_done, r_hi, r_ready = sem("p_hi"), sem("p_ready"), sem("t_done"), sem("r_hi"), sem("r_ready")
        rem_done, gate_done, up_done = sem("rem_done"), sem("gate_done"), sem("up_done")
        silu_done, gu_evac, act_hi, act_ready = sem("silu_done"), sem("gu_evac"), sem("act_hi"), sem("act_ready")
        down_done, dn_hi, dn_ready = sem("down_done"), sem("dn_hi"), sem("dn_ready")
        gl_ready, low_ready, lg_done, gap_ready, exp_done = sem("gl_ready"), sem("low_ready"), sem("lg_done"), sem("gap_ready"), sem("exp_done")
        route_step, route_ready, wt_done = sem("route_step"), sem("route_ready"), sem("wt_done")
        wl_raw, wl_hi, wl_ready = sem("wl_raw"), sem("wl_hi"), sem("wl_ready")
        out_done, out_evac = sem("out_done"), sem("out_evac")
        res_full = [sem("res_full0"), sem("res_full1")]
        stored = [sem("stored0"), sem("stored1")]
        passed = {e: sem(f"passed_{e}") for e in ("pool", "dve", "sp")}
        block = ctx.enter_context(nc.Block())

        def is_low(s):
            return s % SLABS in (S_AGU, S_ADN)

        def arrivals(s):
            return sum(q % RING == s % RING and not is_low(q) for q in range(s + 1))

        ARRIVALS = [sum(q % RING == i and not is_low(q) for q in range(SLABS)) for i in range(RING)]

        def eight(t, n=P):
            return t.rearrange("p (k n) -> p k n", n=n)

        def plane(t, n):
            return t[n] if isinstance(n, int) else t[bass.ds(n, 1)].rearrange("a p n -> (a p) n")

        def tile(t, half, n):
            return t[:, half, n] if isinstance(n, int) else t[:, half, bass.ds(n, 1)].rearrange("p a n -> p (a n)")

        HALVES = ((slice(0, 64), slice(0, TOK // 2)), (slice(64, P), slice(TOK // 2, TOK)))
        OTHERS = ((slice(0, 64), slice(TOK // 2, TOK)), (slice(64, P), slice(0, TOK // 2)))

        @block.sync
        def _(sp):
            for dst, src in ((ids[:], idx), (raw[:, 0, 0:2 * P], c_gu), (raw[0:64, 0, 2 * P:3 * P], c_dn), (idn[:], ident),
                             (col[:], cols), (s16[:], sum16), (io[:], iota), (bias_sb[:], bias),
                             (raw[:, 0, 4 * P:4 * P + KT * EXPERTS], gate_w)):
                sp.dma_start(dst, src).then_inc(const_full, 16)

            def adapters(c):
                return [sp.value_load(idc[0:1, bass.ds(c * 2 + b, 1)], min_val=0, max_val=IDS - 1) for b in range(2)]

            def load_slab(slot, src):
                sp.dma_start(raw[:, slot % RING], src).then_inc(raw_full[slot % RING], 16)

            def load_low(slot, src, which, width):
                for b, a in enumerate(which):
                    sp.dma_start(raw[:, slot % RING, b * width:(b + 1) * width], plane(src, a)).then_inc(low_full, 16)

            sp.wait_ge(const_ready, 1)
            first = adapters(0)
            for k in range(2):
                sp.dma_start(x_stage[:, k], x_t[0, k]).then_inc(xst_full[k], 16)
            load_low(0, a_gu, first, KT * 32)
            load_slab(1, w_stream[W_REM])
            load_slab(2, w_stream[W_GATE])
            for k in range(2, KT):
                sp.wait_ge(x_ready, k - 1)
                sp.dma_start(x_stage[:, k % 2], x_t[0, k]).then_inc(xst_full[k % 2], 16)

            with sp.Fori(0, CHUNKS) as c:
                which = adapters(c)

                def slab_slot_free(s):
                    sp.wait_ge(slab_ready, c * SLABS + (s - (RING - 1)))

                def slabs(count, s, turn=0):
                    for k in range(count):
                        slab_slot_free(turn + (s + k))
                        load_slab(s + k, plane(w_stream, turn + (s + k - (S_REM if s < S_ADN else 2))))

                def load_b(after, src, width):
                    if after is not None:
                        sp.wait_ge(b_ready, c * LB + after)
                    for b, a in enumerate(which):
                        sp.dma_start(b_raw[b * 64:(b + 1) * 64, 0:width], src(a)).then_inc(b_full, 16)

                def b_group(g):
                    return lambda a: b_gu[bass.ds(a, 1), :, bass.ds(g * (GROUP * 256) + 256, GROUP * 256)].rearrange("a p n -> (a p) n")

                load_b(None, lambda a: b_gu[bass.ds(a, 1), :, 0:256].rearrange("a p n -> (a p) n"), 256)
                slabs(2, 3)
                load_b(1, b_group(0), GROUP * 256)
                slabs(7, 5)
                with sp.Fori(0, GROUPS - 2) as g:
                    load_b(g * GROUP + 4, b_group(g + 1), GROUP * 256)
                    slabs(6, 12, g * 6)
                load_b((GROUPS - 2) * GROUP + 4, b_group(GROUPS - 1), GROUP * 256)
                slabs(2, 42)
                slab_slot_free(S_ADN)
                load_low(S_ADN, a_dn, which, (FT + 1) * RANK)
                slabs(3, 45)
                load_b(1 + FT, lambda a: plane(b_dn, a), KT * P)
                slabs(3, 48)
                with sp.Fori(0, KT // 2) as i:
                    for j in range(2):
                        sp.wait_ge(x_ready, c * KT + i * 2 + (KT + j - 1))
                        sp.dma_start(x_stage[:, j], x_t[bass.ds(c + 1, 1), bass.ds(i * 2 + j, 1)].rearrange("a b p n -> (a b p) n"))\
                            .then_inc(xst_full[j], 16)
                        slabs(3, 51 + 3 * j, i * 6)
                sp.wait_ge(b_ready, c * LB + (FT + 1 + KT))
                for b in range(2):
                    sp.dma_start(b_raw[b * 64:(b + 1) * 64, :], lora_b[b * 64:(b + 1) * 64, :]).then_inc(b_full, 16)
                slabs(3, 75)
                slab_slot_free(SLABS)
                load_low(SLABS, a_gu, adapters(c + 1), KT * 32)
                slab_slot_free(SLABS + 1)
                load_slab(SLABS + 1, w_stream[W_REM])
                sp.wait_ge(b_ready, c * LB + LB)
                sp.sem_inc(passed["sp"], 1)
                slab_slot_free(SLABS + 2)
                load_slab(SLABS + 2, w_stream[W_GATE])

        @block.gpsimd
        def _(pool):
            with pool.Fori(0, CHUNKS) as c:
                def stored_by(m):
                    pool.wait_ge(stored[m % 2], c * 64 + 16 * (m // 2))
                    pool.sem_inc(passed["pool"], 1)

                def load_res(m):
                    pool.dma_start(res[:, m % 2], x_t[bass.ds(c, 1), m].rearrange("a p n -> (a p) n")).then_inc(res_full[m % 2], 16)

                def store(m):
                    pool.wait_ge(out_evac, c * KT + (m + 1))
                    pool.sem_inc(passed["pool"], 1)
                    pool.dma_start(out[bass.ds(c, 1), m].rearrange("a p n -> (a p) n"), res[:, m % 2]).then_inc(stored[m % 2], 16)

                load_res(0)
                load_res(1)
                for m in range(0, KT, 2):
                    store(m)
                    store(m + 1)
                    if m + 2 < KT:
                        stored_by(m + 2)
                        load_res(m + 2)
                        stored_by(m + 3)
                        load_res(m + 3)
                stored_by(KT)
                stored_by(KT + 1)
            for i in range(2):
                pool.wait_ge(stored[i], CHUNKS * 64)

        def agu(i, b, half):
            at = b * 64 + half * 32
            return eight(slab[:, i, 0:KT * P])[:, :, at:at + 32]

        def agu_raw(i, b):
            return eight(raw[:, i, b * KT * 32:(b + 1) * KT * 32], 32)

        def adn(i, b, half):
            at = b * 32 + half * 16
            return eight(slab[:, i, 0:(FT + 1) * 64], 64)[:, :, at:at + 16]

        def adn_raw(i, b):
            return eight(raw[:, i, b * (FT + 1) * 16:(b + 1) * (FT + 1) * 16], 16)

        @block.scalar
        def _(ae):
            def rnd(dst, src):
                return ae.activation(dst, src, ACT.Copy)

            ae.wait_ge(const_full, 16 * 9)
            rnd(cgu[:].rearrange("p a n -> p (a n)"), raw[:, 0, 0:2 * P])
            rnd(cdn[:], raw[0:64, 0, 2 * P:3 * P])
            rnd(gw[:, :, 0:EXPERTS], eight(raw[:, 0, 4 * P:4 * P + KT * EXPERTS], EXPERTS)).then_inc(const_hi, 1)

            def hi(c, s, turn=0, per_turn=0):
                i = s % RING
                if is_low(s):
                    low = c * 64 + 32 * (1 + (s == S_ADN) + 2 * (s == SLABS))
                    ae.wait_ge(low_full, low)
                else:
                    ae.wait_ge(raw_full[i], c * (16 * ARRIVALS[i]) + turn * (16 * per_turn // RING) + 16 * arrivals(s))
                if s >= RING:
                    ae.wait_ge(slab_used, c * SLABS + turn * per_turn + (s - (RING - 1)))
                if s % SLABS == S_AGU:
                    rnd(agu(i, 0, 0), agu_raw(i, 0))
                    last = rnd(agu(i, 1, 0), agu_raw(i, 1))
                elif s % SLABS == S_ADN:
                    rnd(adn(i, 0, 0), adn_raw(i, 0))
                    last = rnd(adn(i, 1, 0), adn_raw(i, 1))
                else:
                    last = rnd(slab[:, i, 0:SLAB], raw[:, i])
                last.then_inc(hi_done, 1)

            def x_high(k, stage, use):
                ae.wait_ge(xst_full[stage], use)
                rnd(tile(xs, 0, k), x_stage[:, stage]).then_inc(x_hi, 1)

            def b_high(c, at, width, loads, src=0):
                ae.wait_ge(b_full, c * (B_LOADS * 32) + loads * 32)
                rnd(b_st[:, at:at + width], b_raw[:, src:src + width]).then_inc(b_hi, 1)

            for k in range(2):
                x_high(k, k, 16)
            for s in range(RING):
                hi(0, s)
            for k in range(2, KT):
                x_high(k, k % 2, 16 * (k // 2 + 1))

            with ae.Fori(0, CHUNKS) as c:
                b_high(c, 768, 256, 1)
                ae.wait_ge(slab_used, c * SLABS + 1)
                rnd(phl[:, 0], ps_p[:]).then_inc(p_hi, 1)
                hi(c, 3)
                ae.wait_ge(t_done, c * 2 + 1)
                for w in range(2):
                    for rows, toks in HALVES:
                        last = rnd(r_mv[rows, w, toks], ps_t[w][rows, toks])
                last.then_inc(r_hi, 1)
                hi(c, 4)
                b_high(c, 0, 256, 2)
                ae.wait_ge(rem_done, c + 1)
                ae.activation(s_sb[0:64, :], ps_rem[0:64, :], ACT.Silu).then_inc(silu_done, 1)
                ae.wait_ge(gu_evac, c * GU_EVAC + 2)
                rnd(act_rem[0:64, :], a_sb[0:64, :]).then_inc(act_hi, 1)

                def gu_tile(g, k, last_group):
                    f0 = (GROUPS - 1) * GROUP + k if last_group else k
                    hi(c, 5 + 2 * f0, g, 6)
                    if not (last_group and k == GROUP - 1):
                        nxt = (k + 1) % GROUP
                        ae.wait_ge(b_full, c * (B_LOADS * 32) + g * 32 + 32 * (2 + (f0 + 1) // GROUP))
                        rnd(b_st[:, nxt * 256:(nxt + 1) * 256], b_raw[:, nxt * 256:(nxt + 1) * 256]).then_inc(b_hi, 1)
                    ae.wait_ge(gate_done, c * FT + g * GROUP + (f0 + 1))
                    ae.activation(s_sb[:], bank[2 * k][:], ACT.Silu).then_inc(silu_done, 1)
                    hi(c, 6 + 2 * f0, g, 6)
                    ae.wait_ge(gu_evac, c * GU_EVAC + g * GROUP + (f0 + 4))
                    rnd(tile(act, 0, f0 if last_group else g * GROUP + k), a_sb[:]).then_inc(act_hi, 1)

                with ae.Fori(0, GROUPS - 1) as g:
                    for k in range(GROUP):
                        gu_tile(g, k, False)
                for k in range(GROUP):
                    gu_tile(0, k, True)

                ae.wait_ge(b_full, c * (B_LOADS * 32) + 32 * (B_LOADS - 1))
                ae.wait_ge(slab_used, c * SLABS + (S_ADN + 1))
                rnd(phl[0:64, 0], ps_pd[0:64, :]).then_inc(p_hi, 1)
                hi(c, 47)
                ae.wait_ge(t_done, c * 2 + 2)
                for rows, toks in HALVES:
                    last = rnd(r_mv[rows, 0, toks], ps_td[rows, toks])
                last.then_inc(r_hi, 1)
                with ae.Fori(0, KT // 2) as i:
                    for j in range(2):
                        hi(c, 48 + 3 * j, i, 6)
                        rnd(b_st[:, j * P:(j + 1) * P], b_raw[:, bass.ds(i * 256 + j * P, P)]).then_inc(b_hi, 1)
                        hi(c, 49 + 3 * j, i, 6)
                        x_high(i * 2 + j, j, c * 64 + i * 16 + 80)
                        ae.wait_ge(down_done, c * KT + i * 2 + (j + 1))
                        rnd(tile(dn, 0, i * 2 + j), bank[j][:]).then_inc(dn_hi, 1)
                        hi(c, 50 + 3 * j, i, 6)
                b_high(c, 0, 1024, B_LOADS)
                ae.wait_ge(slab_used, c * SLABS + (S_LOW + 1))
                ae.copy(gl_sb, ps_gl[0:2 * EXPERTS, :]).then_inc(gl_ready, 1)
                ae.copy(s_sb[:], ps_low[:]).then_inc(low_ready, 1)
                hi(c, 72)
                hi(c, 73)
                ae.wait_ge(gap_ready, c + 1)
                ae.activation(wt[:, 1], wt[:, 0], ACT.Exp).then_inc(exp_done, 1)
                hi(c, 74)
                hi(c, 75)
                ae.wait_ge(wl_raw, c + 1)
                rnd(phl[:, 0], a_sb[:]).then_inc(wl_hi, 1)
                for s in range(76, SLABS + RING):
                    hi(c, s)
                ae.wait_ge(out_done, c * KT + KT)

        @block.vector
        def _(ve):
            def low_part(dst, src, high, scale=None):
                return ve.tensor_tensor(dst, src, high.bitcast(fp32), ALU.subtract)

            ve.wait_ge(const_full, 16 * 9)
            ve.tensor_copy(idf[:, 0], ids[:]).then_inc(id_step, 1)
            ve.wait_ge(id_step, 1)
            ve.tensor_scalar(idf[:, 1], idf[:, 0], 0.0, float(IDS), ALU.is_lt, ALU.mult).then_inc(id_step, 1)
            ve.wait_ge(id_step, 2)
            ve.tensor_tensor(idf[:, 0], idf[:, 0], idf[:, 1], ALU.add).then_inc(id_step, 1)
            ve.wait_ge(id_step, 3)
            ve.tensor_scalar(idc[:], idf[:, 0], 0.0, float(IDS - 1), ALU.max, ALU.min)
            ve.wait_ge(const_hi, 1)
            low_part(gw[:, :, EXPERTS:], eight(raw[:, 0, 4 * P:4 * P + KT * EXPERTS], EXPERTS), gw[:, :, 0:EXPERTS])\
                .then_inc(const_ready, 1)

            def lo(c, s, turn=0, per_turn=0):
                i = s % RING
                ve.wait_ge(hi_done, c * SLABS + turn * per_turn + (s + 1))
                if s % SLABS == S_AGU:
                    low_part(agu(i, 0, 1), agu_raw(i, 0), agu(i, 0, 0))
                    last = low_part(agu(i, 1, 1), agu_raw(i, 1), agu(i, 1, 0))
                elif s % SLABS == S_ADN:
                    low_part(adn(i, 0, 1), adn_raw(i, 0), adn(i, 0, 0))
                    last = low_part(adn(i, 1, 1), adn_raw(i, 1), adn(i, 1, 0))
                else:
                    last = low_part(slab[:, i, SLAB:], raw[:, i], slab[:, i, 0:SLAB])
                last.then_inc(slab_ready, 1)

            def x_low(k, stage, n):
                ve.wait_ge(x_hi, n)
                low_part(tile(xs, 1, k), x_stage[:, stage], tile(xs, 0, k)).then_inc(x_ready, 1)

            def b_rows(at, width, count, src):
                ve.wait_ge(b_hi, count)
                b = b_st[:, at:at + width]
                ve.scalar_tensor_tensor(b, b.bitcast(fp32), col[:, 1:2], b_raw[:, src], ALU.mult, ALU.add).then_inc(b_ready, 1)

            def r_rows(w, ps):
                return [ve.scalar_tensor_tensor(r_mv[rows, w, toks], r_mv[rows, w, toks].bitcast(fp32), col[rows, 0:1],
                                                ps[rows, toks], ALU.mult, ALU.add) for rows, toks in HALVES]

            x_low(0, 0, 1)
            x_low(1, 1, 2)
            for s in range(RING):
                lo(0, s)
            for k in range(2, KT):
                x_low(k, k % 2, k + 1)

            with ve.Fori(0, CHUNKS) as c:
                for rows, toks in OTHERS:
                    cleared = ve.memset(r_mv[rows, :, toks].bitcast(fp32), 0.0)
                cleared.then_inc(dn_ready, 1)
                b_rows(768, 256, c * LB + 1, slice(0, 256))
                ve.wait_ge(p_hi, c * 2 + 1)
                low_part(phl[:, 1], ps_p[:], phl[:, 0]).then_inc(p_ready, 1)
                lo(c, 3)
                ve.wait_ge(r_hi, c * 2 + 1)
                r_rows(0, ps_t[0])
                halves = r_rows(1, ps_t[1])
                halves[0].then_inc(gu_evac, 1)
                halves[1].then_inc(r_ready, 1)
                lo(c, 4)
                b_rows(0, 256, c * LB + 2, slice(0, 256))
                ve.wait_ge(silu_done, c * (FT + 1) + 1)
                ve.tensor_tensor(a_sb[0:64, :], s_sb[0:64, :], ps_rem[64:P, :], ALU.mult).then_inc(gu_evac, 1)
                ve.wait_ge(act_hi, c * (FT + 1) + 1)
                low_part(act_rem[64:P, :], a_sb[0:64, :], act_rem[0:64, :]).then_inc(gu_evac, 1)

                def gu_tile(g, k, last_group):
                    f0 = (GROUPS - 1) * GROUP + k if last_group else k
                    lo(c, 5 + 2 * f0, g, 6)
                    if not (last_group and k == GROUP - 1):
                        nxt = (k + 1) % GROUP
                        b_rows(nxt * 256, 256, c * LB + g * GROUP + (f0 + 3), slice(nxt * 256, nxt * 256 + 256))
                    ve.wait_ge(up_done, c * FT + g * GROUP + (f0 + 1))
                    ve.wait_ge(silu_done, c * (FT + 1) + g * GROUP + (f0 + 2))
                    ve.wait_ge(gu_evac, c * GU_EVAC + g * GROUP + (f0 + 3))
                    ve.tensor_tensor(a_sb[:], s_sb[:], bank[2 * k + 1][:], ALU.mult).then_inc(gu_evac, 1)
                    lo(c, 6 + 2 * f0, g, 6)
                    ve.wait_ge(act_hi, c * (FT + 1) + g * GROUP + (f0 + 2))
                    f = f0 if last_group else g * GROUP + k
                    low_part(tile(act, 1, f), a_sb[:], tile(act, 0, f)).then_inc(act_ready, 1)
                    ve.wait_ge(act_ready, c * FT + g * GROUP + (f0 + 1))

                with ve.Fori(0, GROUPS - 1) as g:
                    for k in range(GROUP):
                        gu_tile(g, k, False)
                for k in range(GROUP):
                    gu_tile(0, k, True)

                ve.wait_ge(p_hi, c * 2 + 2)
                low_part(phl[0:64, 1], ps_pd[0:64, :], phl[0:64, 0]).then_inc(p_ready, 1)
                lo(c, 47)
                ve.wait_ge(r_hi, c * 2 + 2)
                halves = r_rows(0, ps_td)
                halves[0].then_inc(dn_ready, 1)
                halves[1].then_inc(r_ready, 1)
                with ve.Fori(0, KT // 2) as i:
                    for j in range(2):
                        lo(c, 48 + 3 * j, i, 6)
                        b_rows(j * P, P, c * LB + i * 2 + (FT + 2 + j), bass.ds(i * 256 + j * P, P))
                        lo(c, 49 + 3 * j, i, 6)
                        x_low(i * 2 + j, j, c * KT + i * 2 + (KT + j + 1))
                        ve.wait_ge(dn_hi, c * KT + i * 2 + (j + 1))
                        low_part(tile(dn, 1, i * 2 + j), bank[j][:], tile(dn, 0, i * 2 + j)).then_inc(dn_ready, 1)
                        lo(c, 50 + 3 * j, i, 6)

                ve.wait_ge(b_hi, c * LB + LB)
                low_part(r_mv[:].rearrange("p a n -> p (a n)"), b_raw[:], b_st[:]).then_inc(b_ready, 1)
                lo(c, 72)
                lo(c, 73)

                steps = [0]

                def step(instruction):
                    steps[0] += 1
                    instruction.then_inc(route_step, 1)
                    ve.wait_ge(route_step, c * ROUTE + steps[0])

                ve.wait_ge(lg_done, c + 1)
                step(ve.tensor_copy(lg[:].rearrange("p a e -> p (a e)"), ps_lg[:, 0:32]))
                ve.sem_inc(passed["dve"], 1)
                for t in range(4):
                    last = ve.max(mx[:, t], lg[:, t])
                step(last)
                ve.tensor_tensor(wt[:, 0], mx[:, :, 1], mx[:, :, 0], ALU.subtract).then_inc(gap_ready, 1)
                for t in range(4):
                    last = ve.max_index(mi[:, t], mx[:, t], lg[:, t])
                step(last)
                step(ve.tensor_copy(mf[:], mi[:]))
                experts = io[:].rearrange("p (a e) -> p a e", a=1).to_broadcast([P, 4, EXPERTS])
                for n in range(2):
                    last = ve.tensor_tensor(eq[:, n], experts, mf[:, :, n:n + 1].to_broadcast([P, 4, EXPERTS]), ALU.is_equal)
                step(last)
                ve.wait_ge(exp_done, c + 1)
                step(ve.tensor_scalar(wt[:, 2], wt[:, 1], 1.0, None, ALU.add))
                step(ve.reciprocal(wt[:, 4], wt[:, 2]))
                step(ve.tensor_scalar(wt[:, 3], wt[:, 4], 2.0, None, ALU.mult))
                step(ve.tensor_tensor(wt[:, 4], wt[:, 3], wt[:, 1], ALU.mult))
                for n in range(2):
                    last = ve.tensor_tensor(eq[:, n], eq[:, n], wt[:, 3 + n].rearrange("p (t a) -> p t a", a=1).to_broadcast([P, 4, EXPERTS]), ALU.mult)
                step(last)
                step(ve.tensor_tensor(eq[:, 0], eq[:, 0], eq[:, 1], ALU.add))
                weights = eq[:, 0].rearrange("p t e -> p (t e)").rearrange("p (e a) -> p e a", a=1).to_broadcast([P, 4 * EXPERTS, RANK])
                ve.tensor_copy(route[:].rearrange("p t e r -> p (t e) r"), weights).then_inc(route_ready, 1)
                assert steps[0] == ROUTE, steps

                lo(c, 74)
                lo(c, 75)
                ve.wait_ge(wt_done, c + 1)
                ve.wait_ge(low_ready, c + 1)
                ve.tensor_tensor(a_sb[:], s_sb[:], ps_wt[:], ALU.mult).then_inc(wl_raw, 1)
                ve.wait_ge(wl_hi, c + 1)
                low_part(phl[:, 1], a_sb[:], phl[:, 0]).then_inc(wl_ready, 1)
                lo(c, 76)

                def evacuate(m):
                    ve.wait_ge(out_done, c * KT + (m + 1))
                    ve.wait_ge(res_full[m % 2], c * 64 + 16 * (m // 2 + 1))
                    ve.scalar_tensor_tensor(res[:, m % 2], bank[4 + m % 4][:], bias_sb[:, m:m + 1], res[:, m % 2],
                                            ALU.add, ALU.add).then_inc(out_evac, 1)

                evacuate(0)
                evacuate(1)
                lo(c, 77)
                evacuate(2)
                evacuate(3)
                lo(c, 78)
                evacuate(4)
                evacuate(5)
                lo(c, 79)
                evacuate(6)
                lo(c, 80)
                evacuate(7)

        @block.tensor
        def _(pe):
            def three(ps, w_hi, w_lo, m_hi, m_lo, start, stop=False):
                pe.matmul(ps, w_hi, m_hi, start=start, stop=False)
                pe.matmul(ps, w_hi, m_lo, start=False, stop=False)
                return pe.matmul(ps, w_lo, m_hi, start=False, stop=stop)

            def slab_tile(i, half, k):
                at = half * SLAB + k * P
                return slab[:, i, at:at + P]

            pe.wait_ge(const_ready, 1)
            with pe.Fori(0, CHUNKS) as c:
                def slab_is_ready(s, turn=0, per_turn=0):
                    pe.wait_ge(slab_ready, c * SLABS + turn * per_turn + (s + 1))

                pe.wait_ge(x_ready, c * KT + KT)
                slab_is_ready(S_AGU)
                for k in range(KT):
                    for half in range(2):
                        last = pe.matmul(ps_p[:], slab[:, S_AGU % RING, k * P:(k + 1) * P], xs[:, half, k],
                                         start=(k + half == 0), stop=(k == KT - 1 and half == 1))
                last.then_inc(slab_used, 1)

                slab_is_ready(S_REM)
                i = S_REM % RING
                for k in range(KT):
                    last = three(ps_rem[:], slab_tile(i, 0, k), slab_tile(i, 1, k), xs[:, 0, k], xs[:, 1, k], k == 0)
                    if k == 5:
                        pe.wait_ge(p_ready, c * 2 + 1)
                        for w in range(2):
                            pe.matmul(ps_t[w][:], cgu[:, w], phl[:, 0], start=True, stop=False)
                            fold = pe.matmul(ps_t[w][:], cgu[:, w], phl[:, 1], start=False, stop=True)
                        fold.then_inc(t_done, 1)
                last.then_inc(slab_used, 1)
                pe.wait_ge(r_ready, c * 2 + 1)
                pe.wait_ge(b_ready, c * LB + 1)
                pe.matmul(ps_rem[:], b_st[:, 768:896], r_mv[:, 0], start=False, stop=False)
                pe.matmul(ps_rem[:], b_st[:, 896:1024], r_mv[:, 1], start=False, stop=True).then_inc(rem_done, 1)

                def gu_tile(g, k, last_group):
                    f0 = (GROUPS - 1) * GROUP + k if last_group else k
                    pe.wait_ge(gu_evac, c * GU_EVAC + g * GROUP + (f0 + 1))
                    for w, done in ((0, gate_done), (1, up_done)):
                        s = S_GATE + 2 * f0 + w
                        slab_is_ready(s, g, 6)
                        i = s % RING
                        ps = bank[2 * k + w][:]
                        for t in range(KT):
                            last = three(ps, slab_tile(i, 0, t), slab_tile(i, 1, t), xs[:, 0, t], xs[:, 1, t], t == 0)
                        last.then_inc(slab_used, 1)
                        if w == 0:
                            pe.wait_ge(b_ready, c * LB + g * GROUP + (f0 + 2))
                        pe.matmul(ps, b_st[:, k * 256 + w * P:k * 256 + (w + 1) * P], r_mv[:, w], start=False, stop=True).then_inc(done, 1)

                with pe.Fori(0, GROUPS - 1) as g:
                    for k in range(GROUP):
                        gu_tile(g, k, False)
                for k in range(GROUP):
                    gu_tile(0, k, True)

                slab_is_ready(S_ADN)
                i = S_ADN % RING
                pe.wait_ge(act_ready, c * FT + (FT - 1))
                for f in range(FT):
                    if f == FT - 1:
                        pe.wait_ge(act_ready, c * FT + FT)
                    for half in range(2):
                        pe.matmul(ps_pd[0:64, :], slab[:, i, f * 64:(f + 1) * 64], act[:, half, f], start=(f + half == 0), stop=False)
                pe.matmul(ps_pd[0:64, :], slab[:, i, FT * 64:(FT + 1) * 64], act_rem[:], start=False, stop=True).then_inc(slab_used, 1)
                pe.wait_ge(p_ready, c * 2 + 2)
                pe.matmul(ps_td[:], cdn[:], phl[0:64, 0], start=True, stop=False)
                pe.matmul(ps_td[:], cdn[:], phl[0:64, 1], start=False, stop=True).then_inc(t_done, 1)

                with pe.Fori(0, KT // 2) as ii:
                    for j in range(2):
                        pe.wait_ge(dn_ready, c * DN + ii * 2 + (j + 1))
                        ps = bank[j][:]
                        for part in range(3):
                            s = S_DOWN + 3 * j + part
                            slab_is_ready(s, ii, 6)
                            i = s % RING
                            for t in range(min(KT, FT - part * KT)):
                                f = part * KT + t
                                last = three(ps, slab_tile(i, 0, t), slab_tile(i, 1, t), act[:, 0, f], act[:, 1, f], f == 0)
                            if part == 2:
                                t += 1
                                pe.matmul(ps, slab_tile(i, 0, t), act_rem[:], start=False, stop=False)
                                last = pe.matmul(ps, slab_tile(i, 1, t), act_rem[:], start=False, stop=False)
                            last.then_inc(slab_used, 1)
                        pe.wait_ge(r_ready, c * 2 + 2)
                        pe.wait_ge(b_ready, c * LB + ii * 2 + (FT + 2 + j))
                        pe.matmul(ps, b_st[:, j * P:(j + 1) * P], r_mv[:, 0], start=False, stop=True).then_inc(down_done, 1)

                slab_is_ready(S_LOW)
                i = S_LOW % RING
                pe.wait_ge(dn_ready, c * DN + (DN - 1))
                for k in range(KT):
                    if k == KT - 1:
                        pe.wait_ge(dn_ready, c * DN + DN)
                    for half in range(2):
                        pe.matmul(ps_gl[0:2 * EXPERTS, :], gw[:, k], dn[:, half, k], start=(k + half == 0), stop=(k == KT - 1 and half == 1))
                    last = three(ps_low[:], slab_tile(i, 0, k), slab_tile(i, 1, k), dn[:, 0, k], dn[:, 1, k], k == 0, k == KT - 1)
                last.then_inc(slab_used, 1)

                def base(m):
                    s = S_BASE + m
                    slab_is_ready(s)
                    i = s % RING
                    if m >= 4:
                        pe.wait_ge(out_evac, c * KT + (m - 3))
                    for k in range(KT):
                        last = three(bank[4 + m % 4][:], slab_tile(i, 0, k), slab_tile(i, 1, k), dn[:, 0, k], dn[:, 1, k], k == 0)
                    last.then_inc(slab_used, 1)

                lora_lo = r_mv[:].rearrange("p a n -> p (a n)")

                def experts(m):
                    cols_m = slice(m * P, (m + 1) * P)
                    three(bank[4 + m % 4][:], b_st[:, cols_m], lora_lo[:, cols_m], phl[:, 0], phl[:, 1], False, True).then_inc(out_done, 1)

                base(0)
                pe.wait_ge(gl_ready, c + 1)
                for t in range(4):
                    last = pe.matmul(ps_lg[:, t * 8:(t + 1) * 8], gl_sb[:, t * P:(t + 1) * P], s16[:], start=True, stop=True)
                last.then_inc(lg_done, 1)
                base(1)
                base(2)
                pe.wait_ge(route_ready, c + 1)
                for t in range(4):
                    last = pe.matmul(ps_wt[:, t * P:(t + 1) * P], route[:, t].rearrange("p e r -> p (e r)"), idn[:], start=True, stop=True)
                last.then_inc(wt_done, 1)
                base(3)
                pe.wait_ge(wl_ready, c + 1)
                pe.wait_ge(b_ready, c * LB + LB)
                for m in range(4):
                    experts(m)
                for m in range(4, KT):
                    base(m)
                    experts(m)


_OUT = (CHUNKS, KT, P, TOK)


def _layouts(x, itok, w_gate, w_up, w_down, a_gate, b_gate, a_up, b_up, a_down, b_down, gate_w, base_w, base_b, lora_a, lora_b):
    def stat(w):
        o, i = w.shape
        return w.reshape(o // P, P, i // P, P).transpose(0, 3, 2, 1)

    whole = FT * P
    gate, up = stat(w_gate[:whole]), stat(w_up[:whole])
    gu = np.stack([gate, up], 1).reshape(2 * FT, P, KT, P)
    rem = stat(np.concatenate([w_gate[whole:], w_up[whole:]]))
    down = np.zeros((H, 3 * SLAB), np.float32)
    down[:, :whole] = w_down[:, :whole]
    down[:, whole:whole + FREM] = down[:, whole + FREM:whole + 2 * FREM] = w_down[:, whole:]
    down = stat(down).reshape(KT, P, 3, KT, P).transpose(0, 2, 1, 3, 4).reshape(3 * KT, P, KT, P)
    low = stat(lora_a.reshape(ER, H))
    w_stream = np.concatenate([rem, gu, down, low, stat(base_w)]).reshape(-1, P, SLAB)

    def a_tiles(a):
        n, r, i = a.shape
        return a.reshape(n, r, i // P, P).transpose(0, 3, 2, 1)

    a_gu = np.concatenate([a_tiles(a_gate[0]), a_tiles(a_up[0])], 3).reshape(IDS, P, KT * 32)
    dnr = a_down[0][:, :, whole:]
    a_dn = a_tiles(np.concatenate([a_down[0][:, :, :whole], dnr, dnr], 2)).reshape(IDS, P, (FT + 1) * RANK)
    bg, bu, bd = (b[0].transpose(0, 2, 1) for b in (b_gate, b_up, b_down))
    b_gu = np.zeros((IDS, RANK, FT + 1, 2, P), np.float32)
    b_gu[:, :, 0, 0, :FREM], b_gu[:, :, 0, 1, FREM:] = bg[:, :, whole:], bu[:, :, whole:]
    b_gu[:, :, 1:, 0], b_gu[:, :, 1:, 1] = bg[:, :, :whole].reshape(IDS, RANK, FT, P), bu[:, :, :whole].reshape(IDS, RANK, FT, P)
    b_gu = np.tile(b_gu.reshape(IDS, RANK, -1), (1, 4, 1))
    b_dn = np.tile(bd, (1, 4, 1))
    x_t = x.reshape(CHUNKS, TOK, KT, P).transpose(0, 2, 3, 1)
    return {
        "w_stream": w_stream, "a_gu": a_gu, "a_dn": a_dn, "b_gu": b_gu, "b_dn": b_dn,
        "lora_b": lora_b.transpose(0, 2, 1).reshape(ER, H),
        "gate_w": gate_w.reshape(EXPERTS, KT, P).transpose(2, 1, 0).reshape(P, KT * EXPERTS),
        "bias": base_b.reshape(KT, P).T,
        "x_t": np.concatenate([x_t, x_t[:1]]),
        "idx": np.concatenate([itok, itok[:2]]).reshape(1, BATCH + 2),
    }


def _constants():
    r = np.arange(P)
    batch, j, rank = r // 64, r // RANK % 4, r % RANK
    q_batch, q_which, q_rank = r // 64, r // RANK % 2, r % RANK
    same = (q_batch[:, None] == batch) & (q_rank[:, None] == rank)
    c_gu = np.concatenate([0.5 * (same & (q_which[:, None] == w)) for w in range(2)], 1)
    d = np.arange(64)
    c_dn = 0.5 * ((d // 32)[:, None] == batch) * ((d % RANK)[:, None] == rank)
    cols = np.stack([-(j % 2), -(j // 2)], 1)
    e = np.arange(EXPERTS)
    sum16 = (np.arange(2 * EXPERTS) % EXPERTS)[:, None] == e
    iota = np.broadcast_to(e, (P, EXPERTS))
    made = {"c_gu": c_gu, "c_dn": c_dn, "ident": np.eye(P), "cols": cols, "sum16": sum16, "iota": iota}
    return {k: v.astype(np.float32) for k, v in made.items()}


def kernel(**inputs):
    import concourse.bacc as _bacc
    from concourse import mybir as _mybir
    from concourse.bass_utils import run_bass_kernel_spmd as _run

    names = ["x", "itok_B_2_6", "L0_cond_W_gate", "L0_cond_W_up", "L0_cond_W_down", "L0_cond_A_gate", "L0_cond_B_gate",
             "L0_cond_A_up", "L0_cond_B_up", "L0_cond_A_down", "L0_cond_B_down", "L0_ffn_gate_w", "L0_ffn_base_w",
             "L0_ffn_base_b", "L0_ffn_lora_A", "L0_ffn_lora_B"]
    arrays = _layouts(*(np.asarray(inputs[n]) for n in names)) | _constants()
    arrays = {k: np.ascontiguousarray(v) for k, v in arrays.items()}
    nc = _bacc.Bacc("TRN2", target_bir_lowering=False, num_devices=1, dynamic_dma_scratch_size=2048)
    args = {k: nc.dram_tensor(f"in_{k}", v.shape, _mybir.dt.from_np(v.dtype), kind="ExternalInput").ap() for k, v in arrays.items()}
    out = nc.dram_tensor("out_0", _OUT, _mybir.dt.float32, kind="ExternalOutput").ap()
    build(nc, **args, out=out)
    r = _run(nc, [{f"in_{k}": v for k, v in arrays.items()}], core_ids=[0])
    got = r.results[0]["out_0"]
    return got.transpose(0, 3, 1, 2).reshape(BATCH, SEQ, H)
```

```python
import concourse.bass as bass
import numpy as np
from concourse import mybir
from contextlib import ExitStack

P = 128
BATCH, SEQ, H = 8, 256, 1024
F = 2752
IDS, RANK = 16, 16
EXPERTS = 8
ER = EXPERTS * RANK
TOK = 512
CHUNKS = BATCH * SEQ // TOK
KT = H // P
FT = F // P
FREM = F - FT * P
GROUP = 3
GROUPS = FT // GROUP
SLAB = KT * P

S_REM, S_AGU = 0, 1
S_GATE = 2
S_ADN = S_GATE + 2 * FT
S_DOWN = S_ADN + 1
S_LOW = S_DOWN + 3 * KT
S_BASE = S_LOW + 1
SLABS = S_BASE + KT
RING = 3
W_REM, W_GATE, W_DOWN = 0, 1, 1 + 2 * FT
W_LOW = W_DOWN + 3 * KT
W_BASE = W_LOW + 1

C_GU, C_DN, C_GATE = 0, 2 * P, 3 * P
K_COL, K_SUM, K_IOTA, K_BIAS = P, P + 2, P + 2 + EXPERTS, P + 2 + 2 * EXPERTS
K_COLS = K_BIAS + KT

LB = 1 + FT + KT + 1
B_LOADS = 1 + GROUPS + 2
GU_EVAC = FT + 5
DN = KT + 2
ROUTE = 11


def build(nc, w_stream, a_gu, a_dn, b_gu, b_dn, lora_b, to_split, kept, x_t, idx, out):
    fp32, f32r, i32, u32 = mybir.dt.float32, mybir.dt.float32r, mybir.dt.int32, mybir.dt.uint32
    ALU, ACT = mybir.AluOpType, mybir.ActivationFunctionType
    ctx = ExitStack()
    with ctx:
        def sb(name, shape, dt):
            return ctx.enter_context(nc.sbuf_tensor(name, shape, dt))

        def sem(name):
            return ctx.enter_context(nc.semaphore(name))

        xs = sb("xs", [P, 2, KT, TOK], f32r)
        dn = sb("dn", [P, 2, KT, TOK], f32r)
        act = sb("act", [P, 2, FT, TOK], f32r)
        act_rem = sb("act_rem", [P, TOK], f32r)
        slab = sb("slab", [P, RING, 2 * SLAB], f32r)
        raw = sb("raw", [P, RING, SLAB], fp32)
        b_raw = sb("b_raw", [P, 1024], fp32)
        b_st = sb("b_st", [P, 1024], f32r)
        r_mv = sb("r_mv", [P, 2, TOK], f32r)
        phl = sb("phl", [P, 2, TOK], f32r)
        x_stage = sb("x_stage", [P, 2, TOK], fp32)
        res = sb("res", [P, 2, TOK], fp32)
        s_sb = sb("s_sb", [P, TOK], fp32)
        a_sb = sb("a_sb", [P, TOK], fp32)
        route = sb("route", [P, 4, EXPERTS, RANK], fp32)
        gl_sb = route[0:2 * EXPERTS].rearrange("p a e r -> p (a e r)")
        cgu = sb("cgu", [P, 2, P], f32r)
        cdn = sb("cdn", [64, P], f32r)
        kept_sb = sb("kept_sb", [P, K_COLS], fp32)
        gw = sb("gw", [P, KT, 2 * EXPERTS], f32r)
        idn = kept_sb[:, 0:P]
        col = kept_sb[:, K_COL:K_COL + 2]
        s16 = kept_sb[0:2 * EXPERTS, K_SUM:K_SUM + EXPERTS]
        io = kept_sb[:, K_IOTA:K_IOTA + EXPERTS]
        bias_sb = kept_sb[:, K_BIAS:K_BIAS + KT]
        lg = sb("lg", [P, 4, 8], fp32)
        mx = sb("mx", [P, 4, 8], fp32)
        mi = sb("mi", [P, 4, 8], u32)
        mf = sb("mf", [P, 4, 8], fp32)
        eq = sb("eq", [P, 2, 4, 8], fp32)
        wt = sb("wt", [P, 5, 4], fp32)
        ids = sb("ids", [1, BATCH + 2], i32)
        idc = sb("idc", [1, BATCH + 2], i32)
        idf = sb("idf", [1, 2, BATCH + 2], fp32)

        bank = [ctx.enter_context(nc.psum_tensor(f"bank{i}", [P, TOK], fp32)) for i in range(8)]
        ps_p, ps_rem, ps_t = bank[2], bank[7], (bank[4], bank[5])
        ps_pd, ps_td = bank[6], bank[7]
        ps_low, ps_gl, ps_lg, ps_wt = bank[2], bank[3], bank[0], bank[1]
        ps_out = [bank[4], bank[5], bank[6], bank[7], bank[2], bank[3], bank[4], bank[5]]

        const_full, idx_full = sem("const_full"), sem("idx_full")
        x0_full = [sem(f"x0_full{k}") for k in range(KT)]
        const_ready, const_hi, id_step = sem("const_ready"), sem("const_hi"), sem("id_step")
        raw_full = [sem(f"raw_full{i}") for i in range(RING)]
        low_full = sem("low_full")
        hi_done, slab_ready, slab_used = sem("hi_done"), sem("slab_ready"), sem("slab_used")
        b_full, b_hi, b_ready = sem("b_full"), sem("b_hi"), sem("b_ready")
        xst_full = [sem("xst_full0"), sem("xst_full1")]
        x_hi, x_ready = sem("x_hi"), sem("x_ready")
        p_done = sem("p_done")
        p_hi, p_ready, t_done, r_hi, r_ready = sem("p_hi"), sem("p_ready"), sem("t_done"), sem("r_hi"), sem("r_ready")
        rem_done, gate_done, up_done = sem("rem_done"), sem("gate_done"), sem("up_done")
        silu_done, gu_evac, act_hi, act_ready = sem("silu_done"), sem("gu_evac"), sem("act_hi"), sem("act_ready")
        down_done, dn_hi, dn_ready = sem("down_done"), sem("dn_hi"), sem("dn_ready")
        gl_ready, low_ready, lg_done, gap_ready, exp_done = sem("gl_ready"), sem("low_ready"), sem("lg_done"), sem("gap_ready"), sem("exp_done")
        route_step, route_ready, wt_done = sem("route_step"), sem("route_ready"), sem("wt_done")
        wl_raw, wl_hi, wl_ready = sem("wl_raw"), sem("wl_hi"), sem("wl_ready")
        out_done, out_evac = sem("out_done"), sem("out_evac")
        res_full = [sem("res_full0"), sem("res_full1")]
        stored = [sem("stored0"), sem("stored1")]
        stored_last = sem("stored_last")
        passed = {e: sem(f"passed_{e}") for e in ("pool", "dve", "sp")}
        block = ctx.enter_context(nc.Block())

        def is_low(s):
            return s % SLABS in (S_AGU, S_ADN)

        def arrivals(s):
            return sum(q % RING == s % RING and not is_low(q) for q in range(s + 1))

        ARRIVALS = [sum(q % RING == i and not is_low(q) for q in range(SLABS)) for i in range(RING)]

        def eight(t, n=P):
            return t.rearrange("p (k n) -> p k n", n=n)

        def plane(t, n):
            return t[n] if isinstance(n, int) else t[bass.ds(n, 1)].rearrange("a p n -> (a p) n")

        def tile(t, half, n):
            return t[:, half, n] if isinstance(n, int) else t[:, half, bass.ds(n, 1)].rearrange("p a n -> p (a n)")

        first_stage = [x_stage[:, 0], x_stage[:, 1], b_raw[:, 0:TOK], b_raw[:, TOK:2 * TOK], s_sb[:], a_sb[:],
                       x_stage[:, 0], x_stage[:, 1]]
        to_split_sb = res[:].rearrange("p a n -> p (a n)")

        HALVES = ((slice(0, 64), slice(0, TOK // 2)), (slice(64, P), slice(TOK // 2, TOK)))
        OTHERS = ((slice(0, 64), slice(TOK // 2, TOK)), (slice(64, P), slice(0, TOK // 2)))

        @block.sync
        def _(sp):
            def adapters(c):
                return [sp.value_load(idc[0:1, bass.ds(c * 2 + b, 1)], min_val=0, max_val=IDS - 1) for b in range(2)]

            def load_slab(slot, src):
                sp.dma_start(raw[:, slot % RING], src).then_inc(raw_full[slot % RING], 16)

            def load_low(slot, src, which, width):
                for b, a in enumerate(which):
                    sp.dma_start(raw[:, slot % RING, b * width:(b + 1) * width], plane(src, a)).then_inc(low_full, 16)

            def first_x(k):
                sp.dma_start(first_stage[k], x_t[0, k]).then_inc(x0_full[k], 16)

            sp.dma_start(ids[:], idx).then_inc(idx_full, 16)
            load_slab(S_REM, w_stream[W_REM])
            for k in range(6):
                first_x(k)
            sp.wait_ge(id_step, 4)
            load_low(S_AGU, a_gu, adapters(0), KT * 32)
            for k in range(6, KT):
                sp.wait_ge(x_ready, k - 5)
                first_x(k)
            load_slab(S_GATE, w_stream[W_GATE])
            sp.dma_start(to_split_sb[:, 0:C_GATE + KT * EXPERTS], to_split).then_inc(const_full, 16)
            sp.dma_start(kept_sb[:], kept).then_inc(const_full, 16)
            sp.wait_ge(x_ready, 4)

            with sp.Fori(0, CHUNKS) as c:
                which = adapters(c)

                def slab_slot_free(s):
                    sp.wait_ge(slab_ready, c * SLABS + (s - (RING - 1)))

                def slabs(count, s, turn=0):
                    for k in range(count):
                        slab_slot_free(turn + (s + k))
                        load_slab(s + k, plane(w_stream, turn + (s + k - (S_GATE - W_GATE if s < S_ADN else S_DOWN - W_DOWN))))

                def load_b(after, src, width):
                    if after is not None:
                        sp.wait_ge(b_ready, c * LB + after)
                    for b, a in enumerate(which):
                        sp.dma_start(b_raw[b * 64:(b + 1) * 64, 0:width], src(a)).then_inc(b_full, 16)

                def b_group(g):
                    return lambda a: b_gu[bass.ds(a, 1), :, bass.ds(g * (GROUP * 256) + 256, GROUP * 256)].rearrange("a p n -> (a p) n")

                load_b(None, lambda a: b_gu[bass.ds(a, 1), :, 0:256].rearrange("a p n -> (a p) n"), 256)
                slabs(2, S_GATE + 1)
                load_b(1, b_group(0), GROUP * 256)
                slabs(7, S_GATE + 3)
                with sp.Fori(0, GROUPS - 2) as g:
                    load_b(g * GROUP + 4, b_group(g + 1), GROUP * 256)
                    slabs(6, S_GATE + 10, g * 6)
                load_b((GROUPS - 2) * GROUP + 4, b_group(GROUPS - 1), GROUP * 256)
                slabs(2, S_ADN - 2)
                slab_slot_free(S_ADN)
                load_low(S_ADN, a_dn, which, (FT + 1) * RANK)
                slabs(3, S_DOWN)
                load_b(1 + FT, lambda a: plane(b_dn, a), KT * P)
                slabs(3, S_DOWN + 3)
                with sp.Fori(0, KT // 2) as i:
                    for j in range(2):
                        sp.wait_ge(x_ready, c * KT + i * 2 + (KT + j - 1))
                        sp.dma_start(x_stage[:, j], x_t[bass.ds(c + 1, 1), bass.ds(i * 2 + j, 1)].rearrange("a b p n -> (a b p) n"))\
                            .then_inc(xst_full[j], 16)
                        slabs(3, S_DOWN + 6 + 3 * j, i * 6)
                sp.wait_ge(b_ready, c * LB + (FT + 1 + KT))
                for b in range(2):
                    sp.dma_start(b_raw[b * 64:(b + 1) * 64, :], lora_b[b * 64:(b + 1) * 64, :]).then_inc(b_full, 16)
                slabs(3, SLABS - 3)
                slab_slot_free(SLABS + S_REM)
                load_slab(SLABS + S_REM, w_stream[W_REM])
                slab_slot_free(SLABS + S_AGU)
                load_low(SLABS + S_AGU, a_gu, adapters(c + 1), KT * 32)
                sp.wait_ge(b_ready, c * LB + LB)
                sp.sem_inc(passed["sp"], 1)
                slab_slot_free(SLABS + 2)
                load_slab(SLABS + 2, w_stream[W_GATE])

        @block.gpsimd
        def _(pool):
            STORES = (KT // 2, KT // 2 - 1)
            pool.wait_ge(const_ready, 1)
            with pool.Fori(0, CHUNKS) as c:
                def stored_by(m):
                    if m == KT + 1:
                        pool.wait_ge(stored_last, c * 16 + 16)
                    else:
                        pool.wait_ge(stored[m % 2], c * (16 * STORES[m % 2]) + 16 * (m // 2))
                    pool.sem_inc(passed["pool"], 1)

                def load_res(m):
                    pool.dma_start(res[:, m % 2], x_t[bass.ds(c, 1), m].rearrange("a p n -> (a p) n")).then_inc(res_full[m % 2], 16)

                def store(m):
                    pool.wait_ge(out_evac, c * KT + (m + 1))
                    pool.sem_inc(passed["pool"], 1)
                    pool.dma_start(out[bass.ds(c, 1), m].rearrange("a p n -> (a p) n"), res[:, m % 2]).then_inc(stored[m % 2], 16)

                load_res(0)
                load_res(1)
                for m in range(0, KT, 2):
                    store(m)
                    if m + 2 < KT:
                        store(m + 1)
                        stored_by(m + 2)
                        load_res(m + 2)
                        stored_by(m + 3)
                        load_res(m + 3)
                stored_by(KT)
                stored_by(KT + 1)
            for i in range(2):
                pool.wait_ge(stored[i], CHUNKS * (16 * STORES[i]))
            pool.wait_ge(stored_last, CHUNKS * 16)

        def agu(i, b, half):
            at = b * 64 + half * 32
            return eight(slab[:, i, 0:KT * P])[:, :, at:at + 32]

        def agu_raw(i, b):
            return eight(raw[:, i, b * KT * 32:(b + 1) * KT * 32], 32)

        def adn(i, b, half):
            at = b * 32 + half * 16
            return eight(slab[:, i, 0:(FT + 1) * 64], 64)[:, :, at:at + 16]

        def adn_raw(i, b):
            return eight(raw[:, i, b * (FT + 1) * 16:(b + 1) * (FT + 1) * 16], 16)

        @block.scalar
        def _(ae):
            def rnd(dst, src):
                return ae.activation(dst, src, ACT.Copy)

            def hi(c, s, turn=0, per_turn=0):
                i = s % RING
                if is_low(s):
                    low = c * 64 + 32 * (1 + (s == S_ADN) + 2 * (s == SLABS + S_AGU))
                    ae.wait_ge(low_full, low)
                else:
                    ae.wait_ge(raw_full[i], c * (16 * ARRIVALS[i]) + turn * (16 * per_turn // RING) + 16 * arrivals(s))
                if s >= RING:
                    ae.wait_ge(slab_used, c * SLABS + turn * per_turn + (s - (RING - 1)))
                if s % SLABS == S_AGU:
                    rnd(agu(i, 0, 0), agu_raw(i, 0))
                    last = rnd(agu(i, 1, 0), agu_raw(i, 1))
                elif s % SLABS == S_ADN:
                    rnd(adn(i, 0, 0), adn_raw(i, 0))
                    last = rnd(adn(i, 1, 0), adn_raw(i, 1))
                else:
                    last = rnd(slab[:, i, 0:SLAB], raw[:, i])
                last.then_inc(hi_done, 1)

            def x_high(k, stage, use):
                ae.wait_ge(xst_full[stage], use)
                rnd(tile(xs, 0, k), x_stage[:, stage]).then_inc(x_hi, 1)

            def b_high(c, at, width, loads, src=0):
                ae.wait_ge(b_full, c * (B_LOADS * 32) + loads * 32)
                rnd(b_st[:, at:at + width], b_raw[:, src:src + width]).then_inc(b_hi, 1)

            def first_x_high(k):
                ae.wait_ge(x0_full[k], 16)
                rnd(xs[:, 0, k], first_stage[k]).then_inc(x_hi, 1)

            hi(0, S_REM)
            for k in range(6):
                first_x_high(k)
            hi(0, S_AGU)
            for k in range(6, KT):
                first_x_high(k)
            hi(0, S_GATE)
            ae.wait_ge(const_full, 16 * 2)
            rnd(cgu[:].rearrange("p a n -> p (a n)"), to_split_sb[:, C_GU:C_GU + 2 * P])
            rnd(cdn[:], to_split_sb[0:64, C_DN:C_DN + P])
            rnd(gw[:, :, 0:EXPERTS], eight(to_split_sb[:, C_GATE:C_GATE + KT * EXPERTS], EXPERTS)).then_inc(const_hi, 1)

            with ae.Fori(0, CHUNKS) as c:
                b_high(c, 768, 256, 1)
                ae.wait_ge(p_done, c * 2 + 1)
                rnd(phl[:, 0], ps_p[:]).then_inc(p_hi, 1)
                hi(c, 3)
                ae.wait_ge(t_done, c * 2 + 1)
                for w in range(2):
                    for rows, toks in HALVES:
                        last = rnd(r_mv[rows, w, toks], ps_t[w][rows, toks])
                last.then_inc(r_hi, 1)
                hi(c, 4)
                b_high(c, 0, 256, 2)

                def gu_tile(g, k, last_group):
                    f0 = (GROUPS - 1) * GROUP + k if last_group else k
                    hi(c, S_GATE + RING + 2 * f0, g, 6)
                    if not (last_group and k == GROUP - 1):
                        nxt = (k + 1) % GROUP
                        ae.wait_ge(b_full, c * (B_LOADS * 32) + g * 32 + 32 * (2 + (f0 + 1) // GROUP))
                        rnd(b_st[:, nxt * 256:(nxt + 1) * 256], b_raw[:, nxt * 256:(nxt + 1) * 256]).then_inc(b_hi, 1)
                    ae.wait_ge(gate_done, c * FT + g * GROUP + (f0 + 1))
                    ae.activation(s_sb[:], bank[2 * k][:], ACT.Silu).then_inc(silu_done, 1)
                    hi(c, S_GATE + 1 + RING + 2 * f0, g, 6)
                    ae.wait_ge(gu_evac, c * GU_EVAC + g * GROUP + (f0 + 4))
                    rnd(tile(act, 0, f0 if last_group else g * GROUP + k), a_sb[:]).then_inc(act_hi, 1)

                with ae.Fori(0, GROUPS - 1) as g:
                    for k in range(GROUP):
                        gu_tile(g, k, False)
                for k in range(GROUP):
                    gu_tile(0, k, True)

                ae.wait_ge(rem_done, c + 1)
                ae.activation(s_sb[0:64, :], ps_rem[0:64, :], ACT.Silu).then_inc(silu_done, 1)
                ae.wait_ge(gu_evac, c * GU_EVAC + GU_EVAC - 1)
                rnd(act_rem[0:64, :], a_sb[0:64, :]).then_inc(act_hi, 1)
                ae.wait_ge(b_full, c * (B_LOADS * 32) + 32 * (B_LOADS - 1))
                ae.wait_ge(p_done, c * 2 + 2)
                rnd(phl[0:64, 0], ps_pd[0:64, :]).then_inc(p_hi, 1)
                hi(c, S_ADN + RING)
                ae.wait_ge(t_done, c * 2 + 2)
                for rows, toks in HALVES:
                    last = rnd(r_mv[rows, 0, toks], ps_td[rows, toks])
                last.then_inc(r_hi, 1)
                with ae.Fori(0, KT // 2) as i:
                    for j in range(2):
                        hi(c, S_DOWN + RING + 3 * j, i, 6)
                        rnd(b_st[:, j * P:(j + 1) * P], b_raw[:, bass.ds(i * 256 + j * P, P)]).then_inc(b_hi, 1)
                        hi(c, S_DOWN + 1 + RING + 3 * j, i, 6)
                        x_high(i * 2 + j, j, c * 64 + i * 16 + 16)
                        ae.wait_ge(down_done, c * KT + i * 2 + (j + 1))
                        rnd(tile(dn, 0, i * 2 + j), bank[j][:]).then_inc(dn_hi, 1)
                        hi(c, S_DOWN + 2 + RING + 3 * j, i, 6)
                b_high(c, 0, 1024, B_LOADS)
                ae.wait_ge(slab_used, c * SLABS + (S_LOW + 1))
                ae.copy(gl_sb, ps_gl[0:2 * EXPERTS, :]).then_inc(gl_ready, 1)
                ae.copy(s_sb[:], ps_low[:]).then_inc(low_ready, 1)
                hi(c, S_LOW + RING)
                hi(c, S_BASE + RING)
                ae.wait_ge(gap_ready, c + 1)
                ae.activation(wt[:, 1], wt[:, 0], ACT.Exp).then_inc(exp_done, 1)
                hi(c, S_BASE + 1 + RING)
                hi(c, S_BASE + 2 + RING)
                ae.wait_ge(wl_raw, c + 1)
                rnd(phl[:, 0], a_sb[:]).then_inc(wl_hi, 1)
                for s in range(S_BASE + 3 + RING, SLABS + RING):
                    hi(c, s)
                ae.wait_ge(out_evac, c * KT + KT)
                ae.dma_start(plane(out[:, KT - 1], c), res[:, (KT - 1) % 2]).then_inc(stored_last, 16)

        @block.vector
        def _(ve):
            def low_part(dst, src, high):
                return ve.tensor_tensor(dst, src, high.bitcast(fp32), ALU.subtract)

            ve.wait_ge(idx_full, 16)
            ve.tensor_copy(idf[:, 0], ids[:]).then_inc(id_step, 1)
            ve.wait_ge(id_step, 1)
            ve.tensor_scalar(idf[:, 1], idf[:, 0], 0.0, float(IDS), ALU.is_lt, ALU.mult).then_inc(id_step, 1)
            ve.wait_ge(id_step, 2)
            ve.tensor_tensor(idf[:, 0], idf[:, 0], idf[:, 1], ALU.add).then_inc(id_step, 1)
            ve.wait_ge(id_step, 3)
            ve.tensor_scalar(idc[:], idf[:, 0], 0.0, float(IDS - 1), ALU.max, ALU.min).then_inc(id_step, 1)

            def lo(c, s, turn=0, per_turn=0):
                i = s % RING
                ve.wait_ge(hi_done, c * SLABS + turn * per_turn + (s + 1))
                if s % SLABS == S_AGU:
                    low_part(agu(i, 0, 1), agu_raw(i, 0), agu(i, 0, 0))
                    last = low_part(agu(i, 1, 1), agu_raw(i, 1), agu(i, 1, 0))
                elif s % SLABS == S_ADN:
                    low_part(adn(i, 0, 1), adn_raw(i, 0), adn(i, 0, 0))
                    last = low_part(adn(i, 1, 1), adn_raw(i, 1), adn(i, 1, 0))
                else:
                    last = low_part(slab[:, i, SLAB:], raw[:, i], slab[:, i, 0:SLAB])
                last.then_inc(slab_ready, 1)

            def x_low(k, stage, n):
                ve.wait_ge(x_hi, n)
                low_part(tile(xs, 1, k), x_stage[:, stage], tile(xs, 0, k)).then_inc(x_ready, 1)

            def b_rows(at, width, count, src):
                ve.wait_ge(b_hi, count)
                b = b_st[:, at:at + width]
                ve.scalar_tensor_tensor(b, b.bitcast(fp32), col[:, 1:2], b_raw[:, src], ALU.mult, ALU.add).then_inc(b_ready, 1)

            def r_rows(w, ps):
                return [ve.scalar_tensor_tensor(r_mv[rows, w, toks], r_mv[rows, w, toks].bitcast(fp32), col[rows, 0:1],
                                                ps[rows, toks], ALU.mult, ALU.add) for rows, toks in HALVES]

            def first_x_low(k):
                ve.wait_ge(x_hi, k + 1)
                low_part(xs[:, 1, k], first_stage[k], xs[:, 0, k]).then_inc(x_ready, 1)

            lo(0, S_REM)
            for k in range(6):
                first_x_low(k)
            lo(0, S_AGU)
            for k in range(6, KT):
                first_x_low(k)
            lo(0, S_GATE)
            ve.wait_ge(const_full, 16 * 2)
            ve.wait_ge(const_hi, 1)
            low_part(gw[:, :, EXPERTS:], eight(to_split_sb[:, C_GATE:C_GATE + KT * EXPERTS], EXPERTS), gw[:, :, 0:EXPERTS])\
                .then_inc(const_ready, 1)

            with ve.Fori(0, CHUNKS) as c:
                for (rows, toks), count in zip(OTHERS, (gu_evac, dn_ready)):
                    ve.memset(r_mv[rows, :, toks].bitcast(fp32), 0.0).then_inc(count, 1)
                b_rows(768, 256, c * LB + 1, slice(0, 256))
                ve.wait_ge(p_hi, c * 2 + 1)
                low_part(phl[:, 1], ps_p[:], phl[:, 0]).then_inc(p_ready, 1)
                lo(c, 3)
                ve.wait_ge(r_hi, c * 2 + 1)
                for half in r_rows(0, ps_t[0]):
                    half.then_inc(gu_evac, 1)
                r_rows(1, ps_t[1])[1].then_inc(r_ready, 1)
                lo(c, 4)
                b_rows(0, 256, c * LB + 2, slice(0, 256))

                def gu_tile(g, k, last_group):
                    f0 = (GROUPS - 1) * GROUP + k if last_group else k
                    lo(c, S_GATE + RING + 2 * f0, g, 6)
                    if not (last_group and k == GROUP - 1):
                        nxt = (k + 1) % GROUP
                        b_rows(nxt * 256, 256, c * LB + g * GROUP + (f0 + 3), slice(nxt * 256, nxt * 256 + 256))
                    ve.wait_ge(up_done, c * FT + g * GROUP + (f0 + 1))
                    ve.wait_ge(silu_done, c * (FT + 1) + g * GROUP + (f0 + 1))
                    ve.tensor_tensor(a_sb[:], s_sb[:], bank[2 * k + 1][:], ALU.mult).then_inc(gu_evac, 1)
                    lo(c, S_GATE + 1 + RING + 2 * f0, g, 6)
                    ve.wait_ge(act_hi, c * (FT + 1) + g * GROUP + (f0 + 1))
                    f = f0 if last_group else g * GROUP + k
                    low_part(tile(act, 1, f), a_sb[:], tile(act, 0, f)).then_inc(act_ready, 1)
                    ve.wait_ge(act_ready, c * FT + g * GROUP + (f0 + 1))

                with ve.Fori(0, GROUPS - 1) as g:
                    for k in range(GROUP):
                        gu_tile(g, k, False)
                for k in range(GROUP):
                    gu_tile(0, k, True)

                ve.wait_ge(silu_done, c * (FT + 1) + (FT + 1))
                ve.tensor_tensor(a_sb[0:64, :], s_sb[0:64, :], ps_rem[64:P, :], ALU.mult).then_inc(gu_evac, 1)
                ve.wait_ge(act_hi, c * (FT + 1) + (FT + 1))
                low_part(act_rem[64:P, :], a_sb[0:64, :], act_rem[0:64, :]).then_inc(gu_evac, 1)
                ve.wait_ge(gu_evac, c * GU_EVAC + GU_EVAC)
                ve.wait_ge(p_hi, c * 2 + 2)
                low_part(phl[0:64, 1], ps_pd[0:64, :], phl[0:64, 0]).then_inc(p_ready, 1)
                lo(c, S_ADN + RING)
                ve.wait_ge(r_hi, c * 2 + 2)
                halves = r_rows(0, ps_td)
                halves[0].then_inc(dn_ready, 1)
                halves[1].then_inc(r_ready, 1)
                with ve.Fori(0, KT // 2) as i:
                    for j in range(2):
                        lo(c, S_DOWN + RING + 3 * j, i, 6)
                        b_rows(j * P, P, c * LB + i * 2 + (FT + 2 + j), bass.ds(i * 256 + j * P, P))
                        lo(c, S_DOWN + 1 + RING + 3 * j, i, 6)
                        x_low(i * 2 + j, j, c * KT + i * 2 + (KT + j + 1))
                        ve.wait_ge(dn_hi, c * KT + i * 2 + (j + 1))
                        low_part(tile(dn, 1, i * 2 + j), bank[j][:], tile(dn, 0, i * 2 + j)).then_inc(dn_ready, 1)
                        lo(c, S_DOWN + 2 + RING + 3 * j, i, 6)

                ve.wait_ge(b_hi, c * LB + LB)
                low_part(r_mv[:].rearrange("p a n -> p (a n)"), b_raw[:], b_st[:]).then_inc(b_ready, 1)
                lo(c, S_LOW + RING)
                lo(c, S_BASE + RING)

                steps = [0]

                def step(instruction):
                    steps[0] += 1
                    instruction.then_inc(route_step, 1)
                    ve.wait_ge(route_step, c * ROUTE + steps[0])

                ve.wait_ge(lg_done, c + 1)
                step(ve.tensor_copy(lg[:].rearrange("p a e -> p (a e)"), ps_lg[:, 0:32]))
                ve.sem_inc(passed["dve"], 1)
                for t in range(4):
                    last = ve.max(mx[:, t], lg[:, t])
                step(last)
                ve.tensor_tensor(wt[:, 0], mx[:, :, 1], mx[:, :, 0], ALU.subtract).then_inc(gap_ready, 1)
                for t in range(4):
                    last = ve.max_index(mi[:, t], mx[:, t], lg[:, t])
                step(last)
                step(ve.tensor_copy(mf[:], mi[:]))
                experts = io.rearrange("p (a e) -> p a e", a=1).to_broadcast([P, 4, EXPERTS])
                for n in range(2):
                    last = ve.tensor_tensor(eq[:, n], experts, mf[:, :, n:n + 1].to_broadcast([P, 4, EXPERTS]), ALU.is_equal)
                step(last)
                ve.wait_ge(exp_done, c + 1)
                step(ve.tensor_scalar(wt[:, 2], wt[:, 1], 1.0, None, ALU.add))
                step(ve.reciprocal(wt[:, 4], wt[:, 2]))
                step(ve.tensor_scalar(wt[:, 3], wt[:, 4], 2.0, None, ALU.mult))
                step(ve.tensor_tensor(wt[:, 4], wt[:, 3], wt[:, 1], ALU.mult))
                for n in range(2):
                    last = ve.tensor_tensor(eq[:, n], eq[:, n], wt[:, 3 + n].rearrange("p (t a) -> p t a", a=1).to_broadcast([P, 4, EXPERTS]), ALU.mult)
                step(last)
                step(ve.tensor_tensor(eq[:, 0], eq[:, 0], eq[:, 1], ALU.add))
                weights = eq[:, 0].rearrange("p t e -> p (t e)").rearrange("p (e a) -> p e a", a=1).to_broadcast([P, 4 * EXPERTS, RANK])
                ve.tensor_copy(route[:].rearrange("p t e r -> p (t e) r"), weights).then_inc(route_ready, 1)
                assert steps[0] == ROUTE, steps

                lo(c, S_BASE + 1 + RING)
                lo(c, S_BASE + 2 + RING)
                ve.wait_ge(wt_done, c + 1)
                ve.wait_ge(low_ready, c + 1)
                ve.tensor_tensor(a_sb[:], s_sb[:], ps_wt[:], ALU.mult).then_inc(wl_raw, 1)
                ve.wait_ge(wl_hi, c + 1)
                low_part(phl[:, 1], a_sb[:], phl[:, 0]).then_inc(wl_ready, 1)
                lo(c, S_BASE + 3 + RING)

                def evacuate(m):
                    ve.wait_ge(out_done, c * KT + (m + 1))
                    ve.wait_ge(res_full[m % 2], c * 64 + 16 * (m // 2 + 1))
                    ve.scalar_tensor_tensor(res[:, m % 2], ps_out[m][:], bias_sb[:, m:m + 1], res[:, m % 2],
                                            ALU.add, ALU.add).then_inc(out_evac, 1)

                evacuate(0)
                evacuate(1)
                lo(c, S_BASE + 4 + RING)
                evacuate(2)
                evacuate(3)
                lo(c, S_BASE + 5 + RING)
                evacuate(4)
                evacuate(5)
                lo(c, S_BASE + 6 + RING)
                evacuate(6)
                lo(c, S_BASE + 7 + RING)
                evacuate(7)

        @block.tensor
        def _(pe):
            def three(ps, w_hi, w_lo, m_hi, m_lo, start, stop=False):
                pe.matmul(ps, w_hi, m_hi, start=start, stop=False)
                pe.matmul(ps, w_hi, m_lo, start=False, stop=False)
                return pe.matmul(ps, w_lo, m_hi, start=False, stop=stop)

            def slab_tile(i, half, k):
                at = half * SLAB + k * P
                return slab[:, i, at:at + P]

            with pe.Fori(0, CHUNKS) as c:
                def slab_is_ready(s, turn=0, per_turn=0):
                    pe.wait_ge(slab_ready, c * SLABS + turn * per_turn + (s + 1))

                def remainder(tiles):
                    for k in tiles:
                        pe.wait_ge(x_ready, c * KT + (k + 1))
                        last = three(ps_rem[:], slab_tile(S_REM, 0, k), slab_tile(S_REM, 1, k), xs[:, 0, k], xs[:, 1, k], k == 0)
                    return last

                slab_is_ready(S_REM)
                remainder(range(0, KT // 2))
                slab_is_ready(S_AGU)
                for k in range(KT):
                    pe.wait_ge(x_ready, c * KT + (k + 1))
                    for half in range(2):
                        last = pe.matmul(ps_p[:], slab[:, S_AGU % RING, k * P:(k + 1) * P], xs[:, half, k],
                                         start=(k + half == 0), stop=(k == KT - 1 and half == 1))
                last.then_inc(p_done, 1)
                remainder(range(KT // 2, KT)).then_inc(slab_used, 1)
                pe.wait_ge(const_hi, 1)
                pe.wait_ge(p_ready, c * 2 + 1)
                pe.matmul(ps_t[0][:], cgu[:, 0], phl[:, 0], start=True, stop=False).then_inc(slab_used, 1)
                pe.matmul(ps_t[0][:], cgu[:, 0], phl[:, 1], start=False, stop=True)
                pe.matmul(ps_t[1][:], cgu[:, 1], phl[:, 0], start=True, stop=False)
                pe.matmul(ps_t[1][:], cgu[:, 1], phl[:, 1], start=False, stop=True).then_inc(t_done, 1)

                def gu_tile(g, k, last_group):
                    f0 = (GROUPS - 1) * GROUP + k if last_group else k
                    pe.wait_ge(gu_evac, c * GU_EVAC + g * GROUP + (f0 + 1))
                    for w, done in ((0, gate_done), (1, up_done)):
                        s = S_GATE + 2 * f0 + w
                        slab_is_ready(s, g, 6)
                        i = s % RING
                        ps = bank[2 * k + w][:]
                        for t in range(KT):
                            last = three(ps, slab_tile(i, 0, t), slab_tile(i, 1, t), xs[:, 0, t], xs[:, 1, t], t == 0)
                        last.then_inc(slab_used, 1)
                        pe.wait_ge(r_ready, c * 2 + 1)
                        if w == 0:
                            pe.wait_ge(b_ready, c * LB + g * GROUP + (f0 + 2))
                        pe.matmul(ps, b_st[:, k * 256 + w * P:k * 256 + (w + 1) * P], r_mv[:, w], start=False, stop=True).then_inc(done, 1)

                with pe.Fori(0, GROUPS - 1) as g:
                    for k in range(GROUP):
                        gu_tile(g, k, False)
                for k in range(GROUP):
                    gu_tile(0, k, True)

                pe.matmul(ps_rem[:], b_st[:, 768:896], r_mv[:, 0], start=False, stop=False)
                pe.matmul(ps_rem[:], b_st[:, 896:1024], r_mv[:, 1], start=False, stop=True).then_inc(rem_done, 1)

                slab_is_ready(S_ADN)
                i = S_ADN % RING
                pe.wait_ge(act_ready, c * FT + (FT - 1))
                for f in range(FT):
                    if f == FT - 1:
                        pe.wait_ge(act_ready, c * FT + FT)
                    for half in range(2):
                        pe.matmul(ps_pd[0:64, :], slab[:, i, f * 64:(f + 1) * 64], act[:, half, f], start=(f + half == 0), stop=False)
                pe.wait_ge(gu_evac, c * GU_EVAC + GU_EVAC)
                pe.matmul(ps_pd[0:64, :], slab[:, i, FT * 64:(FT + 1) * 64], act_rem[:], start=False, stop=True).then_inc(p_done, 1)

                def down_pair(ii, first):
                    for j in range(2):
                        pe.wait_ge(dn_ready, c * DN + ii * 2 + (j + 1))
                        ps = bank[j][:]
                        for part in range(3):
                            s = S_DOWN + 3 * j + part
                            slab_is_ready(s, ii, 6)
                            i = s % RING
                            for t in range(min(KT, FT - part * KT)):
                                f = part * KT + t
                                last = three(ps, slab_tile(i, 0, t), slab_tile(i, 1, t), act[:, 0, f], act[:, 1, f], f == 0)
                                if first and j == 0 and f == KT - 2:
                                    pe.wait_ge(p_ready, c * 2 + 2)
                                    pe.matmul(ps_td[:], cdn[:], phl[0:64, 0], start=True, stop=False).then_inc(slab_used, 1)
                                    pe.matmul(ps_td[:], cdn[:], phl[0:64, 1], start=False, stop=True).then_inc(t_done, 1)
                            if part == 2:
                                t += 1
                                pe.matmul(ps, slab_tile(i, 0, t), act_rem[:], start=False, stop=False)
                                last = pe.matmul(ps, slab_tile(i, 1, t), act_rem[:], start=False, stop=False)
                            last.then_inc(slab_used, 1)
                        pe.wait_ge(r_ready, c * 2 + 2)
                        pe.wait_ge(b_ready, c * LB + ii * 2 + (FT + 2 + j))
                        pe.matmul(ps, b_st[:, j * P:(j + 1) * P], r_mv[:, 0], start=False, stop=True).then_inc(down_done, 1)

                down_pair(0, True)
                with pe.Fori(1, KT // 2) as ii:
                    down_pair(ii, False)

                slab_is_ready(S_LOW)
                pe.wait_ge(const_ready, 1)
                i = S_LOW % RING
                pe.wait_ge(dn_ready, c * DN + (DN - 1))
                for k in range(KT):
                    if k == KT - 1:
                        pe.wait_ge(dn_ready, c * DN + DN)
                    for half in range(2):
                        pe.matmul(ps_gl[0:2 * EXPERTS, :], gw[:, k], dn[:, half, k], start=(k + half == 0), stop=(k == KT - 1 and half == 1))
                    last = three(ps_low[:], slab_tile(i, 0, k), slab_tile(i, 1, k), dn[:, 0, k], dn[:, 1, k], k == 0, k == KT - 1)
                last.then_inc(slab_used, 1)

                def base(m):
                    s = S_BASE + m
                    slab_is_ready(s)
                    i = s % RING
                    if m >= 6:
                        pe.wait_ge(out_evac, c * KT + (m - 5))
                    for k in range(KT):
                        last = three(ps_out[m][:], slab_tile(i, 0, k), slab_tile(i, 1, k), dn[:, 0, k], dn[:, 1, k], k == 0)
                    last.then_inc(slab_used, 1)

                lora_lo = r_mv[:].rearrange("p a n -> p (a n)")

                def experts(m):
                    cols_m = slice(m * P, (m + 1) * P)
                    three(ps_out[m][:], b_st[:, cols_m], lora_lo[:, cols_m], phl[:, 0], phl[:, 1], False, True).then_inc(out_done, 1)

                base(0)
                pe.wait_ge(gl_ready, c + 1)
                for t in range(4):
                    last = pe.matmul(ps_lg[:, t * 8:(t + 1) * 8], gl_sb[:, t * P:(t + 1) * P], s16, start=True, stop=True)
                last.then_inc(lg_done, 1)
                base(1)
                base(2)
                pe.wait_ge(route_ready, c + 1)
                for t in range(4):
                    last = pe.transpose(ps_wt[:, t * P:(t + 1) * P], route[:, t].rearrange("p e r -> p (e r)"), idn)
                last.then_inc(wt_done, 1)
                base(3)
                pe.wait_ge(wl_ready, c + 1)
                pe.wait_ge(b_ready, c * LB + LB)
                for m in range(4):
                    experts(m)
                for m in range(4, KT):
                    base(m)
                    experts(m)


_OUT = (CHUNKS, KT, P, TOK)


def _layouts(x, itok, w_gate, w_up, w_down, a_gate, b_gate, a_up, b_up, a_down, b_down, gate_w, base_w, base_b, lora_a, lora_b):
    def stat(w):
        o, i = w.shape
        return w.reshape(o // P, P, i // P, P).transpose(0, 3, 2, 1)

    whole = FT * P
    gate, up = stat(w_gate[:whole]), stat(w_up[:whole])
    gu = np.stack([gate, up], 1).reshape(2 * FT, P, KT, P)
    rem = stat(np.concatenate([w_gate[whole:], w_up[whole:]]))
    down = np.zeros((H, 3 * SLAB), np.float32)
    down[:, :whole] = w_down[:, :whole]
    down[:, whole:whole + FREM] = down[:, whole + FREM:whole + 2 * FREM] = w_down[:, whole:]
    down = stat(down).reshape(KT, P, 3, KT, P).transpose(0, 2, 1, 3, 4).reshape(3 * KT, P, KT, P)
    low = stat(lora_a.reshape(ER, H))
    w_stream = np.concatenate([rem, gu, down, low, stat(base_w)]).reshape(-1, P, SLAB)

    def a_tiles(a):
        n, r, i = a.shape
        return a.reshape(n, r, i // P, P).transpose(0, 3, 2, 1)

    a_gu = np.concatenate([a_tiles(a_gate[0]), a_tiles(a_up[0])], 3).reshape(IDS, P, KT * 32)
    dnr = a_down[0][:, :, whole:]
    a_dn = a_tiles(np.concatenate([a_down[0][:, :, :whole], dnr, dnr], 2)).reshape(IDS, P, (FT + 1) * RANK)
    bg, bu, bd = (b[0].transpose(0, 2, 1) for b in (b_gate, b_up, b_down))
    b_gu = np.zeros((IDS, RANK, FT + 1, 2, P), np.float32)
    b_gu[:, :, 0, 0, :FREM], b_gu[:, :, 0, 1, FREM:] = bg[:, :, whole:], bu[:, :, whole:]
    b_gu[:, :, 1:, 0], b_gu[:, :, 1:, 1] = bg[:, :, :whole].reshape(IDS, RANK, FT, P), bu[:, :, :whole].reshape(IDS, RANK, FT, P)
    b_gu = np.tile(b_gu.reshape(IDS, RANK, -1), (1, 4, 1))
    b_dn = np.tile(bd, (1, 4, 1))
    c_gu, c_dn, kept = _constants()
    x_t = x.reshape(CHUNKS, TOK, KT, P).transpose(0, 2, 3, 1)
    return {
        "w_stream": w_stream, "a_gu": a_gu, "a_dn": a_dn, "b_gu": b_gu, "b_dn": b_dn,
        "lora_b": lora_b.transpose(0, 2, 1).reshape(ER, H),
        "to_split": np.concatenate([c_gu, c_dn, gate_w.reshape(EXPERTS, KT, P).transpose(2, 1, 0).reshape(P, KT * EXPERTS)], 1),
        "kept": np.concatenate([kept, base_b.reshape(KT, P).T], 1),
        "x_t": np.concatenate([x_t, x_t[:1]]),
        "idx": np.concatenate([itok, itok[:2]]).reshape(1, BATCH + 2),
    }


def _constants():
    r = np.arange(P)
    batch, j, rank = r // 64, r // RANK % 4, r % RANK
    q_batch, q_which, q_rank = r // 64, r // RANK % 2, r % RANK
    same = (q_batch[:, None] == batch) & (q_rank[:, None] == rank)
    c_gu = np.concatenate([0.5 * (same & (q_which[:, None] == w)) for w in range(2)], 1)
    d = np.arange(64)
    c_dn = 0.5 * ((d // 32)[:, None] == batch) * ((d % RANK)[:, None] == rank)
    cols = np.stack([-(j % 2), -(j // 2)], 1)
    e = np.arange(EXPERTS)
    sum16 = (np.arange(2 * EXPERTS) % EXPERTS)[:, None] == e
    iota = np.broadcast_to(e, (P, EXPERTS))
    kept = np.zeros((P, K_BIAS))
    kept[:, :P], kept[:, K_COL:K_COL + 2], kept[:2 * EXPERTS, K_SUM:K_SUM + EXPERTS], kept[:, K_IOTA:K_IOTA + EXPERTS] = np.eye(P), cols, sum16, iota
    c_dn = np.concatenate([c_dn, np.zeros_like(c_dn)])
    return [v.astype(np.float32) for v in (c_gu, c_dn, kept)]


def kernel(**inputs):
    import concourse.bacc as _bacc
    from concourse import mybir as _mybir
    from concourse.bass_utils import run_bass_kernel_spmd as _run

    names = ["x", "itok_B_2_6", "L0_cond_W_gate", "L0_cond_W_up", "L0_cond_W_down", "L0_cond_A_gate", "L0_cond_B_gate",
             "L0_cond_A_up", "L0_cond_B_up", "L0_cond_A_down", "L0_cond_B_down", "L0_ffn_gate_w", "L0_ffn_base_w",
             "L0_ffn_base_b", "L0_ffn_lora_A", "L0_ffn_lora_B"]
    arrays = _layouts(*(np.asarray(inputs[n]) for n in names))
    arrays = {k: np.ascontiguousarray(v) for k, v in arrays.items()}
    nc = _bacc.Bacc("TRN2", target_bir_lowering=False, num_devices=1, dynamic_dma_scratch_size=2048)
    args = {k: nc.dram_tensor(f"in_{k}", v.shape, _mybir.dt.from_np(v.dtype), kind="ExternalInput").ap() for k, v in arrays.items()}
    out = nc.dram_tensor("out_0", _OUT, _mybir.dt.float32, kind="ExternalOutput").ap()
    build(nc, **args, out=out)
    r = _run(nc, [{f"in_{k}": v for k, v in arrays.items()}], core_ids=[0])
    got = r.results[0]["out_0"]
    return got.transpose(0, 3, 1, 2).reshape(BATCH, SEQ, H)
```
